# Optimizing a Trainium2 kernel written in Bass

```python
import numpy as np
import jax
import jax.numpy as jnp

def _softmax(x, axis=-1):
    return jax.nn.softmax(x, axis=axis)
def _gelu(x):
    return jax.nn.gelu(x, approximate=True)
def _silu(x):
    return jax.nn.silu(x)
def _sigmoid(x):
    return jax.nn.sigmoid(x)
def _layernorm(x, axis=-1, eps=1e-5):
    m = jnp.mean(x, axis=axis, keepdims=True)
    v = jnp.var(x, axis=axis, keepdims=True)
    return (x - m) / jnp.sqrt(v + eps)
def _scatter_add(tgt, idx, src, axis=0):
    return tgt.at[idx].add(src)
def _segment_sum(src, seg, n):
    return jax.ops.segment_sum(src, seg, n)

kernel_name = 'mk_metaformer_d1_conv_nhwc256_08c02d'

def setup_inputs(seed: int = 0):
    np.random.seed(seed)
    _w = jnp.asarray
    def _rec_inputs():
        import jax
        import jax.numpy as jnp
        _gk = jax.random.key(seed)
        x = 7.22e-05 + 1 * jax.random.normal(jax.random.fold_in(_gk, 1), (8, 64, 64, 256), jnp.float32)
        return x
    x = _rec_inputs()
    def _L0_conv_setup():
        import jax, jax.numpy as jnp
        import numpy as np
        key = jax.random.key(seed)
        ks = jax.random.split(key, 5)
        B, H, W, C = (8, 64, 64, 256)
        C8 = C // 8
        s = 0.05
        return {'x': jax.random.normal(ks[0], (B, H, W, C), dtype=jnp.float32), 'Wq': jax.random.normal(ks[1], (C, C8), dtype=jnp.float32) * s, 'bq': jnp.zeros((C8,), dtype=jnp.float32), 'Wk': jax.random.normal(ks[2], (C, C8), dtype=jnp.float32) * s, 'bk': jnp.zeros((C8,), dtype=jnp.float32), 'Wv': jax.random.normal(ks[3], (C, C8), dtype=jnp.float32) * s, 'bv': jnp.zeros((C8,), dtype=jnp.float32), 'Wo': jax.random.normal(ks[4], (C8, C), dtype=jnp.float32) * s, 'bo': jnp.zeros((C,), dtype=jnp.float32)}
    _L0_conv_all = _L0_conv_setup()
    _L0_conv_in = {k: v for k, v in _L0_conv_all.items() if k in ('Wq', 'bq', 'Wk', 'bk', 'Wv', 'bv', 'Wo', 'bo', )}
    del _L0_conv_all

    def _L0_ffn_setup():
        import jax, jax.numpy as jnp
        import numpy as np
        from jax import lax
        key = jax.random.key(seed)
        B, T, I, H = (64, 2048, 256, 256)
        ks = jax.random.split(key, 13)
        s = 1.0 / np.sqrt(H)

        def w(k, shape):
            return jax.random.uniform(k, shape, jnp.float32, -s, s)
        return {'x': jax.random.normal(ks[0], (B, T, I), jnp.float32), 'U_i': w(ks[1], (I, H)), 'V_i': w(ks[2], (H, H)), 'b_i': w(ks[3], (H,)), 'U_f': w(ks[4], (I, H)), 'V_f': w(ks[5], (H, H)), 'b_f': w(ks[6], (H,)), 'U_c': w(ks[7], (I, H)), 'V_c': w(ks[8], (H, H)), 'b_c': w(ks[9], (H,)), 'U_o': w(ks[10], (I, H)), 'V_o': w(ks[11], (H, H)), 'b_o': w(ks[12], (H,))}
    _L0_ffn_all = _L0_ffn_setup()
    _L0_ffn_in = {k: v for k, v in _L0_ffn_all.items() if k in ('U_i', 'V_i', 'b_i', 'U_f', 'V_f', 'b_f', 'U_c', 'V_c', 'b_c', 'U_o', 'V_o', 'b_o', )}
    del _L0_ffn_all

    return {
        "x": x,
        "L0_conv_Wq": _L0_conv_in["Wq"],
        "L0_conv_bq": _L0_conv_in["bq"],
        "L0_conv_Wk": _L0_conv_in["Wk"],
        "L0_conv_bk": _L0_conv_in["bk"],
        "L0_conv_Wv": _L0_conv_in["Wv"],
        "L0_conv_bv": _L0_conv_in["bv"],
        "L0_conv_Wo": _L0_conv_in["Wo"],
        "L0_conv_bo": _L0_conv_in["bo"],
        "L0_ffn_U_i": _L0_ffn_in["U_i"],
        "L0_ffn_V_i": _L0_ffn_in["V_i"],
        "L0_ffn_b_i": _L0_ffn_in["b_i"],
        "L0_ffn_U_f": _L0_ffn_in["U_f"],
        "L0_ffn_V_f": _L0_ffn_in["V_f"],
        "L0_ffn_b_f": _L0_ffn_in["b_f"],
        "L0_ffn_U_c": _L0_ffn_in["U_c"],
        "L0_ffn_V_c": _L0_ffn_in["V_c"],
        "L0_ffn_b_c": _L0_ffn_in["b_c"],
        "L0_ffn_U_o": _L0_ffn_in["U_o"],
        "L0_ffn_V_o": _L0_ffn_in["V_o"],
        "L0_ffn_b_o": _L0_ffn_in["b_o"],
    }

def reference(x, L0_conv_Wq, L0_conv_bq, L0_conv_Wk, L0_conv_bk, L0_conv_Wv, L0_conv_bv, L0_conv_Wo, L0_conv_bo, L0_ffn_U_i, L0_ffn_V_i, L0_ffn_b_i, L0_ffn_U_f, L0_ffn_V_f, L0_ffn_b_f, L0_ffn_U_c, L0_ffn_V_c, L0_ffn_b_c, L0_ffn_U_o, L0_ffn_V_o, L0_ffn_b_o):
    import jax
    import jax.numpy as jnp
    def _L0_conv_ref(x, Wq, bq, Wk, bk, Wv, bv, Wo, bo):
        import jax, jax.numpy as jnp
        import numpy as np
        B, H, W, C = x.shape
        C8 = C // 8
        N = H * W
        q = jax.nn.relu(jnp.einsum('bhwc,cd->bhwd', x, Wq) + bq).reshape(B, N, C8)
        k = jax.nn.relu(jnp.einsum('bhwc,cd->bhwd', x, Wk) + bk).reshape(B, N, C8)
        v = jax.nn.relu(jnp.einsum('bhwc,cd->bhwd', x, Wv) + bv).reshape(B, N, C8)
        attn = jax.nn.softmax(jnp.einsum('bnd,bmd->bnm', q, k), axis=-1)
        out = jnp.einsum('bnm,bmd->bnd', attn, v).reshape(B, H, W, C8)
        out = jax.nn.relu(jnp.einsum('bhwd,dc->bhwc', out, Wo) + bo)
        return out

    def _L0_ffn_ref(x, U_i, V_i, b_i, U_f, V_f, b_f, U_c, V_c, b_c, U_o, V_o, b_o):
        import jax, jax.numpy as jnp
        import numpy as np
        from jax import lax
        B, T, _ = x.shape
        H = U_i.shape[1]
        xt = jnp.swapaxes(x, 0, 1)
        xi = xt @ U_i + b_i
        xf = xt @ U_f + b_f
        xg = xt @ U_c + b_c
        xo = xt @ U_o + b_o
        h0 = jnp.zeros((B, H), x.dtype)
        c0 = jnp.zeros((B, H), x.dtype)

        def step(carry, xs):
            h, c = carry
            xi_t, xf_t, xg_t, xo_t = xs
            i_t = jax.nn.sigmoid(xi_t + h @ V_i)
            f_t = jax.nn.sigmoid(xf_t + h @ V_f)
            g_t = jnp.tanh(xg_t + h @ V_c)
            o_t = jax.nn.sigmoid(xo_t + h @ V_o)
            c_new = h * c + i_t * g_t
            h_new = o_t * jnp.tanh(c_new)
            return ((h_new, c_new), h_new)
        (_, _), hs = lax.scan(step, (h0, c0), (xi, xf, xg, xo))
        return jnp.swapaxes(hs, 0, 1)

    def _gn(v, G=32, eps=1e-5):
        B_, H_, W_, C_ = v.shape
        g = v.reshape(B_, H_, W_, G, C_ // G)
        m = jnp.mean(g, axis=(1, 2, 4), keepdims=True)
        s = jnp.var(g, axis=(1, 2, 4), keepdims=True)
        return ((g - m) / jnp.sqrt(s + eps)).reshape(v.shape)

    def _ln_c(v, eps=1e-6):
        m = jnp.mean(v, axis=-1, keepdims=True)
        s = jnp.var(v, axis=-1, keepdims=True)
        return (v - m) / jnp.sqrt(s + eps)

    def _ln_t(v, eps=1e-5):
        m = jnp.mean(v, axis=-1, keepdims=True)
        s = jnp.var(v, axis=-1, keepdims=True)
        return (v - m) / jnp.sqrt(s + eps)

    def _to_tokens(v):
        B_, H_, W_, C_ = v.shape
        return v.reshape(B_, H_ * W_, C_)
    def _from_tokens(t, like):
        return t.reshape(like.shape)

    x = x + _L0_conv_ref(_ln_c(x), L0_conv_Wq, L0_conv_bq, L0_conv_Wk, L0_conv_bk, L0_conv_Wv, L0_conv_bv, L0_conv_Wo, L0_conv_bo)
    t = _to_tokens(x)
    t = t + _L0_ffn_ref(_ln_t(t), L0_ffn_U_i, L0_ffn_V_i, L0_ffn_b_i, L0_ffn_U_f, L0_ffn_V_f, L0_ffn_b_f, L0_ffn_U_c, L0_ffn_V_c, L0_ffn_b_c, L0_ffn_U_o, L0_ffn_V_o, L0_ffn_b_o)
    x = _from_tokens(t, x)
    return x


_drawn_inputs = setup_inputs


def setup_inputs(seed=0):
    import zlib

    import numpy as np

    out = dict(_drawn_inputs(seed))
    spreads = {'L0_conv_bq': (0.0, 0.8),
     'L0_conv_bk': (0.0, 0.8),
     'L0_conv_bv': (0.0, 0.766),
     'L0_conv_bo': (0.0, 0.1)}
    factors = {'L0_conv_Wq': 4.074,
     'L0_conv_Wk': 3.858,
     'L0_conv_Wv': 3.624,
     'L0_ffn_V_i': 8.0,
     'L0_ffn_b_i': 24.352,
     'L0_ffn_V_c': 3.828,
     'L0_ffn_b_c': 6.969,
     'L0_ffn_V_o': 8.0,
     'L0_ffn_b_o': 8.0}
    for name, (base, spread) in spreads.items():
        noise = np.random.default_rng([zlib.crc32(name.encode()), seed]).standard_normal(out[name].shape)
        drawn = base * np.exp(spread * noise) if base else spread * noise
        out[name] = jnp.asarray(drawn.astype(out[name].dtype))
    for name, factor in factors.items():
        out[name] = (out[name] * factor).astype(out[name].dtype)
    return out
```

```python
import concourse.bass as bass
from concourse import mybir
from contextlib import ExitStack


def metaformer_layer(nc, x, Wq, bq, Wk, bk, Wv, bv, Wo, bo,
                     U_i, V_i, b_i, U_f, V_f, b_f, U_c, V_c, b_c, U_o, V_o, b_o, out):
    f32, h16, i32 = mybir.dt.float32, mybir.dt.float16, mybir.dt.int32
    ALU, ACT, AX = mybir.AluOpType, mybir.ActivationFunctionType, mybir.AxisListType

    B, HH, WW, C = x.shape
    T = HH * WW
    D = Wq.shape[1]
    P = 128
    KC = C // P
    BLOCKS = T // P
    UNITS = B * BLOCKS
    STEPS = P // B
    LBLOCKS = T // STEPS
    AHEAD = B + 2
    CH = 512
    CHUNKS = T // CH
    SUB = CH // P
    GROUP = 4
    GROUPS = UNITS // GROUP
    QK = 3 * D
    QR = QK + 2
    ONE = 32768.0
    Z = 32.0
    EPS_C, EPS_T = 1e-6, 1e-5
    PEAK_PE = [1, 3, 4, 6, 8, 11, 12, 13]
    PEAK_DVE = [2, 4, 6, 8, 10, 12, 13, 14]
    SCORE = [0, 2, 4, 6, 7, 10, 12, 14]
    MIX = {s: [(s // 2, (0, 1))] if s % 2 else [(s // 2 - 1, (2, 3))] for s in range(1, STEPS)}
    MIX[8], MIX[9] = [(3, (2, 3)), (4, (0,))], [(4, (1,))]
    GATE_PE = {9: 13, 10: 5, 11: 5, 12: 1, 13: 5, 14: 6, 15: 7}

    xt = x.rearrange("b h w c -> (b h w) c").rearrange("(n p) c -> n p c", p=P)
    xg = x.rearrange("b h w c -> (b h w) c").rearrange("(g j p) c -> g p j c", p=P, j=GROUP)
    out_steps = out.rearrange("b h w c -> b (h w) c").rearrange("b (i t) c -> i t b c", t=STEPS)
    mixed = nc.dram_tensor("mixed", (B * T, C), f32).ap()
    mixed_tiles = mixed.rearrange("(n p) c -> n p c", p=P)
    mixed_steps = mixed.rearrange("(b i t) c -> i t b c", b=B, t=STEPS)

    def tile_of(u):
        return (u % B) * BLOCKS + (u // B) % BLOCKS

    ctx = ExitStack()
    with ctx:
        def sb(name, shape, dt=f32):
            return ctx.enter_context(nc.sbuf_tensor(name, shape, dt))

        def sem(name):
            return ctx.enter_context(nc.semaphore(name))

        def two(name):
            return [sem(name + "_even"), sem(name + "_odd")]

        bank = [ctx.enter_context(nc.psum_tensor(f"bank{i}", [P, 512], f32)) for i in range(8)]
        z_ig, z_o = bank[0:2], bank[2:4]
        peak_ps, score_ps, mix_ps, misc = bank[4], bank[5], bank[6], bank[7]

        V_raw, U_raw = sb("V_raw", [P, KC, 3, C]), sb("U_raw", [P, KC, 3, C])
        V_hi, V_lo = sb("V_hi", [P, KC, 3 * C], h16), sb("V_lo", [P, KC, 3 * C], h16)
        U_hi, U_lo = sb("U_hi", [P, KC, 3 * C], h16), sb("U_lo", [P, KC, 3 * C], h16)
        bias_raw = sb("bias_raw", [1, 3, C])
        bias_lo = sb("bias_lo", [1, 3 * C], h16)
        bias_parts = sb("bias_parts", [2, 3 * C], h16)
        ones2 = sb("ones2", [2, P], h16)
        W_raw = sb("W_raw", [P, KC, 3, D])
        Wq_hi, Wq_lo = sb("Wq_hi", [P, KC, QK], h16), sb("Wq_lo", [P, KC, QK], h16)
        Wk_hi, Wk_lo = sb("Wk_hi", [P, KC, QK], h16), sb("Wk_lo", [P, KC, QK], h16)
        Wv_hi, Wv_lo = sb("Wv_hi", [P, KC, D], h16), sb("Wv_lo", [P, KC, D], h16)
        bqk_raw = sb("bqk_raw", [QK, 2])
        bqk = sb("bqk", [QK, 2])
        bv_all, bo_all = sb("bv_all", [P, D]), sb("bo_all", [P, C])
        Wo_x = sb("Wo_x", [D + 1, C + 1])
        ident = sb("ident", [P, P])
        minus_half, eps = sb("minus_half", [P, GROUP]), sb("eps", [P, 2, GROUP])
        bn_seen = sb("bn_seen", [P, 1])
        peaks, tops, pow2 = sb("peaks", [P, 8]), sb("tops", [P, 8]), sb("pow2", [P, 8])
        rec2, sc = sb("rec2", [P, 8]), sb("sc", [P, 16])
        span, inv_r, r_pow = sb("span", [P, 2]), sb("inv_r", [P, 2]), sb("r_pow", [P, 2])
        U_by, b_by, x_by, ones_by = (sb(name, [P, 1]) for name in ("U_by", "b_by", "x_by", "ones_by"))

        keys = sb("keys", [P, B * T], h16)
        vals = sb("vals", [P, UNITS, D + 1])
        edge = sb("edge", [P - QK, CH], h16)
        g_x, g_n = sb("g_x", [P, 2, GROUP, C]), sb("g_n", [P, 2, GROUP, C])
        g_hi, g_lo = sb("g_hi", [P, 2, KC, CH], h16), sb("g_lo", [P, 2, KC, CH], h16)
        g_bn, g_mv = sb("g_bn", [P, GROUP, 6]), sb("g_mv", [P, 2, GROUP, 2])
        g_rstd, g_shift, g_kf, g_vf = sb("g_rstd", [P, 2, GROUP]), sb("g_shift", [P, 2, GROUP]), sb("g_kf", [QK, CH]), sb("g_vf", [P, GROUP, D])

        u_x, u_res, u_out = sb("u_x", [P, 2, C]), sb("u_res", [P, 2, C]), sb("u_out", [P, 2, C])
        u_v = sb("u_v", [P, 2, BLOCKS, D + 1])
        u_bn, u_mv, u_rstd = sb("u_bn", [P, 6]), sb("u_mv", [P, 2]), sb("u_rstd", [P, 1])
        u_n = sb("u_n", [P, C])
        u_hi, u_lo = sb("u_hi", [P, KC, P], h16), sb("u_lo", [P, KC, P], h16)
        q_f = sb("q_f", [QK, P])
        q_stack = sb("q_stack", [P, 2, P], h16)
        q_peak = sb("q_peak", [P, P], h16)
        chunk_max, neg_max, max_hi = sb("chunk_max", [P, CHUNKS]), sb("neg_max", [P, 1]), sb("max_hi", [P, 1], h16)
        max_cols = sb("max_cols", [P, P])
        probs = sb("probs", [P, 2, CH])
        mix_t = sb("mix_t", [D + 1, P])
        rsum, att = sb("rsum", [P, 1]), sb("att", [P, C])

        l_x = sb("l_x", [P, 2, C])
        l_n = sb("l_n", [P, C])
        l_bn, l_mv, l_rstd = sb("l_bn", [P, 6]), sb("l_mv", [P, 2]), sb("l_rstd", [P, 1])
        l_hi, l_lo = sb("l_hi", [P, KC, P], h16), sb("l_lo", [P, KC, P], h16)
        S = KC * B
        cell = sb("cell", [P, 2, 2, S, 4])
        scan = sb("scan", [P, S, 4])
        t_o, t_c = sb("t_o", [P, 2, S]), sb("t_c", [P, S])
        h_hi, h_lo = sb("h_hi", [P, S], h16), sb("h_lo", [P, S], h16)
        h_all = sb("h_all", [P, 2, KC, STEPS, B])
        y_out = sb("y_out", [P, 2, C])

        loaded, wo_loaded, ident_ready, const_ready = sem("loaded"), sem("wo_loaded"), sem("ident_ready"), sem("const_ready")
        chain = sem("dve_chain")
        span_ready, roots_ready = sem("span_ready"), sem("roots_ready")
        tops_in, tops_out, weights_ready, bias_low, bias_moved = (
            sem("tops_in"), sem("tops_out"), sem("weights_ready"), sem("bias_low"), sem("bias_moved"))
        g_loaded = two("g_loaded")
        g_shifted, g_normed, g_turned, g_hi_done, g_lo_done = (
            sem("g_shifted"), sem("g_normed"), sem("g_turned"), sem("g_hi_done"), sem("g_lo_done"))
        g_k_proj, g_v_proj, g_relu, g_keys, g_vals = (
            sem("g_k_proj"), sem("g_v_proj"), sem("g_relu"), sem("g_keys"), sem("g_vals"))

        x_loaded, v_loaded, res_loaded = two("x_loaded"), two("v_loaded"), two("res_loaded")
        u_normed, u_turned, u_hi_done, u_lo_done = sem("u_normed"), sem("u_turned"), sem("u_hi_done"), sem("u_lo_done")
        q_proj, q_relu, q_ready = sem("q_proj"), sem("q_relu"), sem("q_ready")
        peak_scored, peak_read, max_ready, max_turned, max_rows, q_copied = (
            sem("peak_scored"), sem("peak_read"), sem("max_ready"), sem("max_turned"), sem("max_rows"), sem("q_copied"))
        scored, exp_done, mixed_chunk, mix_copied, projected, u_ready, u_stored = (
            sem("scored"), sem("exp_done"), sem("mixed_chunk"), sem("mix_copied"), sem("projected"),
            sem("u_ready"), sem("u_stored"))

        l_loaded, y_stored = two("l_loaded"), two("y_stored")
        l_normed, l_turned, l_hi_done, l_lo_done, l_proj = (
            sem("l_normed"), sem("l_turned"), sem("l_hi_done"), sem("l_lo_done"), sem("l_proj"))
        ig_ready, o_ready, ig_act, c_ready, c_act = (
            sem("ig_ready"), sem("o_ready"), sem("ig_act"), sem("c_ready"), sem("c_act"))
        h_hi_ready, h_ready, h_lo_ready, hc_ready = sem("h_hi_ready"), sem("h_ready"), sem("h_lo_ready"), sem("hc_ready")
        h_turned, y_ready = sem("h_turned"), sem("y_ready")
        edge_ready, edge_rows = sem("edge_ready"), sem("edge_rows")
        g_stats, g_rstd_ready, u_stats, u_rstd_ready, l_stats, l_rstd_ready = (
            sem("g_stats"), sem("g_rstd_ready"), sem("u_stats"), sem("u_rstd_ready"), sem("l_stats"), sem("l_rstd_ready"))
        u_chain, q_chain, m_chain, l_chain, tail_chain, g_chain = (
            sem("u_chain"), sem("q_chain"), sem("m_chain"), sem("l_chain"), sem("tail_chain"), sem("g_chain"))

        def wait(eng, s, value):
            if not isinstance(value, int) or value > 0:
                eng.wait_ge(s, value)

        def schedule(eng, iteration):
            A = AHEAD // 2
            F = LBLOCKS // 2 + A
            iteration(-1, 0, {"front"})
            iteration(-1, 1, {"front", "peak"})
            units = {"front", "peak", "mix"}
            iteration(0, 0, units)
            iteration(0, 1, units | {"tail"})
            units |= {"tail"}
            with eng.Fori(1, A - 1) as k:
                iteration(k, 0, units)
                iteration(k, 1, units)
            iteration(A - 1, 0, units)
            iteration(A - 1, 1, units | {"prepare"})
            both = units | {"prepare", "steps"}
            iteration(A, 0, both)
            iteration(A, 1, both | {"output"})
            both |= {"output"}
            with eng.Fori(A + 1, UNITS // 2) as k:
                iteration(k, 0, both)
                iteration(k, 1, both)
            last = {"prepare", "steps", "output"}
            iteration(UNITS // 2, 0, last | {"tail"})
            iteration(UNITS // 2, 1, last)
            with eng.Fori(UNITS // 2 + 1, F - 1) as k:
                iteration(k, 0, last)
                iteration(k, 1, last)
            iteration(F - 1, 0, last)
            iteration(F - 1, 1, last - {"prepare"})
            iteration(F, 0, {"output"})

        def later(k, p, n):
            return k + (p + n) // 2, (p + n) % 2

        def slots(eng, slot):
            for g in range(-3, 2):
                slot(g // 2, g % 2, 3)
            with eng.Fori(1, GROUPS // 2 - 2) as k:
                slot(k, 0, 3)
                slot(k, 1, 3)
            for g in range(GROUPS - 4, GROUPS + 1):
                slot(g // 2, g % 2, GROUPS - 1 - g)

        def has(k, p, n, after):
            return n <= after and (not isinstance(k, int) or 2 * k + p + n >= 0)

        def parity_count(k, p, d):
            return k + (p + d) // 2

        block = ctx.enter_context(nc.Block())

        @block.sync
        def _(sp):
            for g, (v, u, b) in enumerate(((V_i, U_i, b_i), (V_c, U_c, b_c), (V_o, U_o, b_o))):
                sp.dma_start(V_raw[:, :, g, :], v.rearrange("(k p) n -> p k n", p=P)).then_inc(loaded, 16)
                sp.dma_start(U_raw[:, :, g, :], u.rearrange("(k p) n -> p k n", p=P)).then_inc(loaded, 16)
                sp.dma_start(bias_raw[:, g, :], b.rearrange("(a n) -> a n", a=1)).then_inc(loaded, 16)
            for g, w in enumerate((Wq, Wk, Wv)):
                sp.dma_start(W_raw[:, :, g, :], w.rearrange("(k p) n -> p k n", p=P)).then_inc(loaded, 16)
            for r in range(3):
                for g, b in enumerate((bq, bk)):
                    sp.dma_start(bqk_raw[r * D:(r + 1) * D, g:g + 1], b.rearrange("(n a) -> n a", a=1)).then_inc(loaded, 16)
            sp.dma_start(bv_all[:, :], bv.rearrange("(a n) -> a n", a=1).broadcast_to((P, D))).then_inc(loaded, 16)
            sp.dma_start(bo_all[:, :], bo.rearrange("(a n) -> a n", a=1).broadcast_to((P, C))).then_inc(loaded, 16)
            sp.wait_ge(const_ready, 1)
            sp.dma_start(Wo_x[0:D, 1:C + 1], Wo).then_inc(wo_loaded, 16)
            sp.wait_ge(edge_ready, 1)
            sp.dma_start(keys[QK:P, :].rearrange("p (g c) -> p g c", c=CH),
                         edge[:, :].unsqueeze(1).broadcast_to((P - QK, GROUPS, CH))).then_inc(edge_rows, 16)
            sp.wait_ge(bias_low, 1)
            sp.dma_start(bias_parts[1:2, :], bias_lo[:, :]).then_inc(bias_moved, 16)

            def group(k, p):
                g = 2 * k + p
                wait(sp, g_normed, g - 1)
                sp.dma_start(g_x[:, p, :, :], xg[g]).then_inc(g_loaded[p], 16)

            group(0, 0)
            group(0, 1)
            with sp.Fori(1, GROUPS // 2) as k:
                group(k, 0)
                group(k, 1)
            sp.wait_ge(g_vals, GROUPS)

            sp.dma_start(u_x[:, 0, :], xt[tile_of(0)]).then_inc(x_loaded[0], 16)

            def iteration(k, p, parts):
                u = 2 * k + p
                q = 1 - p
                stored = 16 * (u - 1)
                if "front" in parts:
                    if not isinstance(k, int) or u + 1 >= 0:
                        wait(sp, mixed_chunk, CHUNKS * u)
                        sp.dma_start(u_v[:, q, :, :], vals[:, bass.ds(((u + 1) % B) * BLOCKS, BLOCKS), :]).then_inc(v_loaded[q], 16)
                    wait(sp, u_normed, u + 2)
                    sp.dma_start(u_x[:, q, :], xt[tile_of(u + 3)]).then_inc(x_loaded[q], 16)
                if "mix" in parts:
                    wait(sp, u_ready, u - 1)
                    sp.dma_start(u_res[:, p, :], xt[tile_of(u)]).then_inc(res_loaded[p], 16)
                i = u - AHEAD
                if "output" in parts:
                    sp.wait_ge(y_ready, i)
                    sp.dma_start(out_steps[i - 1], y_out[:, q, :]).then_inc(y_stored[q], 16)
                if "prepare" in parts:
                    sp.wait_ge(u_stored, stored if "mix" in parts or "tail" in parts else 16 * UNITS)
                    sp.dma_start(l_x[:, q, :], mixed_steps[i + 1]).then_inc(l_loaded[q], 16)
                if "tail" in parts:
                    wait(sp, u_stored, stored)
                    sp.wait_ge(u_ready, u)
                    sp.dma_start(mixed_tiles[tile_of(u - 1)], u_out[:, q, :]).then_inc(u_stored, 16)

            schedule(sp, iteration)
            for p in range(2):
                sp.wait_ge(y_stored[p], 16 * LBLOCKS // 2)
            sp.wait_ge(u_stored, 16 * UNITS)

        @block.gpsimd
        def _(pool):
            pool.memset(Wo_x[:, :], 0.0).then_inc(ident_ready, 1)
            pool.wait_ge(ident_ready, 1)
            pool.memset(Wo_x[D:D + 1, 0:1], 1.0).then_inc(const_ready, 1)
            pool.wait_ge(const_ready, 1)
            pool.memset(ident[:, :], 0.0).then_inc(ident_ready, 1)
            pool.wait_ge(ident_ready, 2)
            pool.affine_select(out=ident[:, :], in_=ident[:, :], compare_op=ALU.not_equal, fill=1.0,
                               base=0, pattern=[[-1, P]], channel_multiplier=1).then_inc(ident_ready, 1)
            pool.wait_ge(ident_ready, 3)
            pool.memset(ones2[:, :], 1.0).then_inc(ident_ready, 1)
            pool.wait_ge(ident_ready, 4)
            pool.memset(minus_half[:, :], -0.5)
            pool.memset(eps[:, 0, :], EPS_C)
            pool.memset(eps[:, 1, :], EPS_T)
            pool.memset(vals[:, :, D:D + 1], 1.0).then_inc(ident_ready, 1)
            pool.wait_ge(ident_ready, 5)
            pool.memset(max_cols[:, :], 0.0).then_inc(ident_ready, 1)
            pool.wait_ge(ident_ready, 6)
            pool.memset(q_stack[QK:P, :, :], 0.0).then_inc(ident_ready, 1)
            pool.wait_ge(ident_ready, 7)
            pool.memset(edge[:, :], 0.0).then_inc(ident_ready, 1)
            pool.wait_ge(ident_ready, 8)
            pool.memset(edge[0:QR - QK, :], ONE).then_inc(edge_ready, 1)
            pool.wait_ge(edge_ready, 1)
            pool.wait_ge(tops_in, 1)
            pool.partition_all_reduce(tops[:, :], peaks[:, :], P, bass.bass_isa.ReduceOp.max).then_inc(tops_out, 1)
            pool.wait_ge(span_ready, 1)
            pool.tensor_tensor(inv_r[:, :], span[:, :], minus_half[:, 0:2], ALU.pow).then_inc(roots_ready, 1)

            def root(n, out, mv, which, signal, steps=2):
                pool.tensor_tensor(out, mv, eps[:, which, 0:out.shape[1]], ALU.add).then_inc(signal, 1)
                pool.wait_ge(signal, steps * n + 1)
                pool.tensor_tensor(out, out, minus_half[:, 0:out.shape[1]], ALU.pow).then_inc(signal, 1)

            def slot(k, p, after):
                if has(k, p, 3, after):
                    h, q = later(k, p, 3)
                    g = 2 * h + q
                    pool.wait_ge(g_stats, g + 1)
                    wait(pool, g_normed, g - 1)
                    root(g, g_rstd[:, q, :], g_mv[:, q, :, 1], 0, g_rstd_ready)

            slots(pool, slot)

            def iteration(k, p, parts):
                u = 2 * k + p
                i = u - AHEAD
                if "front" in parts:
                    pool.wait_ge(u_stats, u + 3)
                    root(u + 2, u_rstd[:, :], u_mv[:, 1:2], 0, u_rstd_ready)
                if "prepare" in parts:
                    pool.wait_ge(l_stats, i + 2)
                    root(i + 1, l_rstd[:, :], l_mv[:, 1:2], 1, l_rstd_ready, 3)
                    pool.wait_ge(l_rstd_ready, 3 * (i + 1) + 2)
                    pool.tensor_tensor(l_rstd[:, :], l_rstd[:, :], x_by[:, :], ALU.mult).then_inc(l_rstd_ready, 1)

            schedule(pool, iteration)

        @block.vector
        def _(dve):
            V = nc.vector
            links = [0]

            def link(ins):
                links[0] += 1
                ins.then_inc(chain, 1)
                dve.wait_ge(chain, links[0])

            dve.wait_ge(loaded, 16 * 20)
            dve.wait_ge(ident_ready, 5)
            link(V.memset(peaks[:, :], 0.0))

            def biggest(col, a, axis, rows=P):
                V.tensor_reduce(peaks[0:rows, col:col + 1], a, axis, ALU.max, apply_absolute_value=True)

            biggest(0, V_raw[:, :, :, :], AX.XYZ)
            biggest(1, U_raw[:, :, :, :], AX.XYZ)
            biggest(2, bias_raw[:, :, :], AX.XY, 1)
            biggest(3, W_raw[:, :, 0, :], AX.XY)
            biggest(4, W_raw[:, :, 1, :], AX.XY)
            biggest(5, W_raw[:, :, 2, :], AX.XY)
            biggest(6, bqk_raw[:, 0:1], AX.X, QK)
            V.tensor_reduce(peaks[0:QK, 7:8], bqk_raw[:, 1:2], AX.X, ALU.max, apply_absolute_value=True).then_inc(tops_in, 1)
            dve.wait_ge(tops_out, 1)
            V.tensor_scalar(span[:, :], tops[:, 1:3], 2.0 ** -20, None, ALU.max).then_inc(span_ready, 1)
            dve.wait_ge(roots_ready, 1)
            link(V.tensor_scalar(inv_r[:, :].bitcast(i32), inv_r[:, :].bitcast(i32), 0x7F800000, None, ALU.bitwise_and))
            link(V.reciprocal(r_pow[:, :], inv_r[:, :]))
            for scale, a, factor in ((U_by, inv_r[:, 0:1], Z / 4), (x_by, r_pow[:, 0:1], 4.0),
                                     (b_by, inv_r[:, 1:2], Z / 4), (ones_by, r_pow[:, 1:2], 4.0)):
                link(V.tensor_scalar(scale[:, :], a, factor, None, ALU.mult))
            link(V.memset(sc[:, :], 1.0))
            link(V.tensor_reduce(sc[:, 1:2], tops[:, 3:6], AX.X, ALU.max))
            link(V.scalar_tensor_tensor(sc[:, 2:4], tops[:, 3:5], float(C), tops[:, 6:8], ALU.mult, ALU.add))
            link(V.tensor_scalar(sc[:, 0:4], sc[:, 0:4], 1e-30, None, ALU.max))
            link(V.tensor_scalar(pow2[:, 0:4].bitcast(i32), sc[:, 0:4].bitcast(i32), 0x7F800000, None, ALU.bitwise_and))
            link(V.reciprocal(rec2[:, 0:4], pow2[:, 0:4]))
            link(V.tensor_scalar(sc[:, 4:6], rec2[:, 0:2], 2.0 ** 12, None, ALU.mult))
            link(V.tensor_scalar(sc[:, 6:8], pow2[:, 0:2], 2.0 ** -12, None, ALU.mult))
            link(V.tensor_scalar(sc[:, 8:10], rec2[:, 2:4], 2.0 ** 11, None, ALU.mult))
            link(V.tensor_scalar(sc[:, 10:12], sc[:, 8:10], sc[:, 7:8], None, ALU.mult))
            link(V.tensor_scalar(sc[:, 12:13], pow2[:, 2:3], pow2[:, 3:4], 2.0 ** -22, ALU.mult, ALU.mult))
            link(V.tensor_tensor(bqk[:, :], bqk_raw[:, :], sc[0:QK, 8:10], ALU.mult))

            def split(hi, lo, raw, factor):
                link(V.tensor_scalar(raw, raw, factor, None, ALU.mult))
                link(V.tensor_copy(hi, raw))
                link(V.tensor_tensor(lo, raw, hi, ALU.subtract))

            for g, (hi, lo) in enumerate(((Wq_hi, Wq_lo), (Wk_hi, Wk_lo), (Wv_hi, Wv_lo))):
                split(hi[:, :, 0:D], lo[:, :, 0:D], W_raw[:, :, g, :], sc[:, 5:6])
                for r in range(1, hi.shape[2] // D):
                    link(V.tensor_copy(hi[:, :, r * D:(r + 1) * D], hi[:, :, 0:D]))
                    link(V.tensor_copy(lo[:, :, r * D:(r + 1) * D], lo[:, :, 0:D]))
            for g, half in ((0, 0.5), (1, 1.0), (2, 0.5)):
                link(V.tensor_scalar(V_raw[:, :, g, :], V_raw[:, :, g, :], half * 0.5 * Z, None, ALU.mult))
                link(V.tensor_scalar(U_raw[:, :, g, :], U_raw[:, :, g, :], half, None, ALU.mult))
                link(V.tensor_scalar(bias_raw[:, g, :], bias_raw[:, g, :], half, None, ALU.mult))
            link(V.tensor_copy(V_hi[:, :, :], V_raw[:, :, :, :].rearrange("p k g n -> p k (g n)")))
            link(V.tensor_tensor(V_lo[:, :, :], V_raw[:, :, :, :].rearrange("p k g n -> p k (g n)"), V_hi[:, :, :], ALU.subtract))
            split(U_hi[:, :, :], U_lo[:, :, :], U_raw[:, :, :, :].rearrange("p k g n -> p k (g n)"), U_by[:, :])
            bias = bias_raw[:, :, :].rearrange("p g n -> p (g n)")
            link(V.tensor_scalar(bias, bias, b_by[0:1, :], None, ALU.mult))
            link(V.tensor_copy(bias_parts[0:1, :], bias))
            link(V.tensor_scalar(ones2[:, :], ones2[:, :], ones_by[0:2, :], None, ALU.mult))
            V.tensor_tensor(bias_lo[:, :], bias, bias_parts[0:1, :], ALU.subtract).then_inc(bias_low, 1)
            link(V.memset(cell[:, :, :, :, :], 1.0))
            link(V.memset(cell[:, :, 1, :, 0], 0.0))
            V.memset(cell[:, 0, 0, :, 3], 0.0).then_inc(hc_ready, 1)
            V.memset(h_lo[:, :], 0.0).then_inc(h_lo_ready, 1)
            V.memset(h_hi[:, :], 0.0).then_inc(h_hi_ready, 1)
            link(V.memset(scan[:, :, :], 0.0))
            V.memset(t_c[:, :], 0.0).then_inc(weights_ready, 1)

            def stats(k, p):
                g = 2 * k + p
                dve.wait_ge(g_loaded[p], 16 * (k + 1))
                for j in range(GROUP):
                    last = V.bn_stats(g_bn[:, j, :], g_x[:, p, j, :])
                last.then_inc(g_chain, 1)
                dve.wait_ge(g_chain, g + 1)
                V.tensor_copy(bn_seen[:, :], g_bn[:, 0, 0:1])
                for j in range(GROUP):
                    last = V.bn_aggr(g_mv[:, p, j, :], g_bn[:, j, :])
                last.then_inc(g_stats, 1)

            def shift(k, p):
                g = 2 * k + p
                dve.wait_ge(g_rstd_ready, 2 * (g + 1))
                wait(dve, g_normed, g - 1)
                V.scalar_tensor_tensor(g_shift[:, p, :], g_mv[:, p, :, 0], -1.0, g_rstd[:, p, :],
                                       ALU.mult, ALU.mult).then_inc(g_shifted, 1)

            def low_parts(k, p):
                g = 2 * k + p
                dve.wait_ge(g_hi_done, g + 1)
                for c in range(KC):
                    last = V.tensor_tensor(g_lo[:, p, c, :], (z_ig, z_o)[p][c][:, :], g_hi[:, p, c, :], ALU.subtract)
                last.then_inc(g_lo_done, 1)

            def store_keys(k, p):
                g = 2 * k + p
                dve.wait_ge(g_relu, g + 1)
                V.tensor_copy(keys[0:QK, bass.ds(g * CH, CH)], g_kf[:, :]).then_inc(g_keys, 1)
                dve.wait_ge(g_keys, 2 * g + 1)
                low = keys[2 * D:QK, bass.ds(g * CH, CH)]
                V.tensor_tensor(low, g_kf[2 * D:QK, :], low, ALU.subtract).then_inc(g_keys, 1)
                dve.wait_ge(g_v_proj, g + 1)
                v_ps = (misc, mix_ps)[p][:, 0:GROUP * D].rearrange("p (j n) -> p j n", n=D)
                V.scalar_tensor_tensor(g_vf[:, :, :], v_ps, sc[:, 7:8], bv_all[:, :].unsqueeze(1).broadcast_to((P, GROUP, D)),
                                       ALU.mult, ALU.add).then_inc(g_vals, 1)
                dve.wait_ge(g_vals, 2 * g + 1)
                V.tensor_scalar(vals[:, bass.ds(g * GROUP, GROUP), 0:D], g_vf[:, :, :], 0.0, None, ALU.max).then_inc(g_vals, 1)

            def slot(k, p, after):
                if has(k, p, -1, after):
                    store_keys(*later(k, p, -1))
                if has(k, p, 2, after):
                    shift(*later(k, p, 2))
                if has(k, p, 1, after):
                    low_parts(*later(k, p, 1))
                if has(k, p, 3, after):
                    stats(*later(k, p, 3))

            slots(dve, slot)

            def iteration(k, p, parts):
                u = 2 * k + p
                q = 1 - p
                i = u - AHEAD

                def piece(s):
                    if s == 0 and "front" in parts:
                        dve.wait_ge(x_loaded[p], 16 * (k + 2))
                        V.bn_stats(u_bn[:, :], u_x[:, p, :]).then_inc(u_chain, 1)
                        dve.wait_ge(u_chain, u + 3)
                        V.tensor_copy(bn_seen[:, :], u_bn[:, 0:1])
                        V.bn_aggr(u_mv[:, :], u_bn[:, :]).then_inc(u_stats, 1)
                    if s == 1 and "output" in parts:
                        dve.wait_ge(h_turned, i)
                        wait(dve, y_stored[q], 16 * (parity_count(k, p, -1) - AHEAD // 2))
                        V.scalar_tensor_tensor(y_out[:, q, :], misc[:, 0:C], 0.5, l_x[:, q, :],
                                               ALU.mult, ALU.add).then_inc(y_ready, 1)
                    if s == 1 and "front" in parts:
                        dve.wait_ge(u_rstd_ready, 2 * (u + 3))
                        wait(dve, u_turned, u + 2)
                        V.tensor_scalar(u_n[:, :], u_x[:, p, :], u_mv[:, 0:1], u_rstd[:, :],
                                        ALU.subtract, ALU.mult).then_inc(u_normed, 1)
                    if s == 3 and "tail" in parts:
                        dve.wait_ge(projected, u)
                        V.reciprocal(rsum[:, :], misc[:, 0:1]).then_inc(tail_chain, 1)
                        dve.wait_ge(tail_chain, 2 * u - 1)
                        V.scalar_tensor_tensor(att[:, :], misc[:, 1:C + 1], rsum[:, :], bo_all[:, :],
                                               ALU.mult, ALU.add).then_inc(tail_chain, 1)
                    if s == 11 and "tail" in parts:
                        dve.wait_ge(tail_chain, 2 * u)
                        dve.wait_ge(res_loaded[q], 16 * (parity_count(k, p, -1) + 1))
                        wait(dve, u_stored, 16 * (u - 2))
                        V.scalar_tensor_tensor(u_out[:, q, :], att[:, :], 0.0, u_res[:, q, :],
                                               ALU.max, ALU.add).then_inc(u_ready, 1)
                    if s == 5 and "front" in parts:
                        dve.wait_ge(u_hi_done, u + 3)
                        V.tensor_tensor(u_lo[:, :, :].rearrange("p k n -> p (k n)"), misc[:, 0:C],
                                        u_hi[:, :, :].rearrange("p k n -> p (k n)"), ALU.subtract).then_inc(u_lo_done, 1)
                    if s == 7 and "front" in parts:
                        dve.wait_ge(q_relu, u + 3)
                        V.tensor_copy(q_stack[0:QK, p, :], q_f[:, :]).then_inc(q_chain, 1)
                        dve.wait_ge(q_chain, u + 3)
                        low = q_stack[D:2 * D, p, :]
                        V.tensor_tensor(low, q_f[D:2 * D, :], low, ALU.subtract).then_inc(q_ready, 1)
                    if s == 5 and "prepare" in parts:
                        dve.wait_ge(l_loaded[q], 16 * (parity_count(k, p, 1) + 1 - AHEAD // 2))
                        V.bn_stats(l_bn[:, :], l_x[:, q, :]).then_inc(l_chain, 1)
                    if s == 6 and "prepare" in parts:
                        dve.wait_ge(l_chain, i + 2)
                        V.tensor_copy(bn_seen[:, :], l_bn[:, 0:1])
                        V.bn_aggr(l_mv[:, :], l_bn[:, :]).then_inc(l_stats, 1)
                    if s == 7 and "prepare" in parts:
                        dve.wait_ge(l_rstd_ready, 3 * (i + 2))
                        V.tensor_scalar(l_n[:, :], l_x[:, q, :], l_mv[:, 0:1], l_rstd[:, :],
                                        ALU.subtract, ALU.mult).then_inc(l_normed, 1)
                    if s == 9 and "prepare" in parts:
                        dve.wait_ge(l_hi_done, i + 2)
                        V.tensor_tensor(l_lo[:, :, :].rearrange("p k n -> p (k n)"), misc[:, 0:C],
                                        l_hi[:, :, :].rearrange("p k n -> p (k n)"), ALU.subtract).then_inc(l_lo_done, 1)
                    if s in PEAK_DVE and "peak" in parts:
                        c = PEAK_DVE.index(s)
                        dve.wait_ge(peak_scored, CHUNKS * (u + 1) + c + 1)
                        V.tensor_reduce(chunk_max[:, c:c + 1], peak_ps[:, :], AX.X, ALU.max).then_inc(peak_read, 1)
                    if s == STEPS - 1 and "peak" in parts:
                        dve.wait_ge(peak_read, CHUNKS * (u + 2))
                        V.tensor_reduce(neg_max[:, :], chunk_max[:, :], AX.X, ALU.max, negate=True).then_inc(m_chain, 1)
                        dve.wait_ge(m_chain, 2 * (u + 1) + 1)
                        V.tensor_scalar(max_cols[:, QK:QK + 1], neg_max[:, :], 1.0 / ONE, None, ALU.mult)
                        V.tensor_scalar(max_hi[:, :], neg_max[:, :], 1.0 / ONE, None, ALU.mult).then_inc(m_chain, 1)
                        dve.wait_ge(m_chain, 2 * (u + 1) + 2)
                        V.scalar_tensor_tensor(max_cols[:, QK + 1:QR], neg_max[:, :], 1.0 / ONE, max_hi[:, :],
                                               ALU.mult, ALU.subtract).then_inc(max_ready, 1)
                        if "mix" in parts:
                            dve.wait_ge(scored, CHUNKS * (u + 1))
                        V.tensor_copy(q_peak[0:QK, :], q_stack[0:QK, q, :]).then_inc(q_copied, 1)

                def step(s):
                    n = STEPS * i + s
                    dve.wait_ge(ig_act, n + 1)
                    dve.wait_ge(hc_ready, n + 1)
                    flat = "p e r -> p (e r)"
                    V.tensor_tensor_scan(scan[:, :, :].rearrange(flat), cell[:, s % 2, 0, :, :].rearrange(flat),
                                         cell[:, s % 2, 1, :, :].rearrange(flat), 0.0, ALU.add, ALU.mult).then_inc(c_ready, 1)
                    dve.wait_ge(c_act, n + 1)
                    two_h = h_all[:, p, :, s, :]
                    o_v = t_o[:, s % 2, :].rearrange("p (k b) -> p k b", b=B)
                    c_v = t_c[:, :].rearrange("p (k b) -> p k b", b=B)
                    V.scalar_tensor_tensor(h_hi[:, :], t_o[:, s % 2, :], 1.0, t_c[:, :], ALU.add, ALU.mult).then_inc(h_hi_ready, 1)
                    V.scalar_tensor_tensor(two_h, o_v, 1.0, c_v, ALU.add, ALU.mult).then_inc(h_ready, 1)
                    dve.wait_ge(h_ready, n + 1)
                    V.tensor_tensor(h_lo[:, :].rearrange("p (k b) -> p k b", b=B), two_h,
                                    h_hi[:, :].rearrange("p (k b) -> p k b", b=B), ALU.subtract).then_inc(h_lo_ready, 1)
                    V.scalar_tensor_tensor(cell[:, (s + 1) % 2, 0, :, 3].rearrange("p (k b) -> p k b", b=B), two_h, 0.5,
                                           scan[:, :, 3].rearrange("p (k b) -> p k b", b=B), ALU.mult, ALU.mult).then_inc(hc_ready, 1)

                for s in range(STEPS):
                    piece(s)
                    if "steps" in parts:
                        step(s)

            schedule(dve, iteration)

        @block.scalar
        def _(act):
            A = nc.scalar
            act.wait_ge(weights_ready, 1)
            A.activation(t_o[:, 0, :], t_c[:, :], ACT.Exp)

            def turn(k, p):
                g = 2 * k + p
                act.wait_ge(g_turned, g + 1)
                wait(act, g_k_proj, g - 1)
                wait(act, g_v_proj, g - 1)
                for c in range(KC):
                    last = A.activation(g_hi[:, p, c, :], (z_ig, z_o)[p][c][:, :], ACT.Copy)
                last.then_inc(g_hi_done, 1)

            def relu_keys(k, p):
                g = 2 * k + p
                act.wait_ge(g_k_proj, g + 1)
                wait(act, g_keys, 2 * g)
                A.activation(g_kf[:, :], (score_ps, peak_ps)[p][0:QK, :], ACT.Relu, bias=bqk[:, 1:2],
                             scale=sc[0:QK, 11:12]).then_inc(g_relu, 1)

            def normalise(k, p):
                g = 2 * k + p
                act.wait_ge(g_shifted, g + 1)
                wait(act, g_turned, g - 1)
                for j in range(GROUP):
                    last = A.activation(g_n[:, p, j, :], g_x[:, p, j, :], ACT.Identity, bias=g_shift[:, p, j:j + 1],
                                        scale=g_rstd[:, p, j:j + 1])
                last.then_inc(g_normed, 1)

            def slot(k, p, after):
                if has(k, p, 1, after):
                    turn(*later(k, p, 1))
                if has(k, p, 2, after):
                    normalise(*later(k, p, 2))
                if has(k, p, 0, after):
                    relu_keys(k, p)

            slots(act, slot)

            def iteration(k, p, parts):
                u = 2 * k + p
                i = u - AHEAD

                def piece(s):
                    if s in SCORE and "mix" in parts:
                        c = SCORE.index(s)
                        act.wait_ge(scored, CHUNKS * u + c + 1)
                        wait(act, mixed_chunk, CHUNKS * u + c - 1)
                        A.activation(probs[:, c % 2, :], score_ps[:, :], ACT.Exp, scale=sc[:, 12:13]).then_inc(exp_done, 1)
                    if s == 0 and "tail" in parts:
                        act.wait_ge(mixed_chunk, CHUNKS * u)
                        A.activation(mix_t[:, :], mix_ps[0:D + 1, 0:P], ACT.Copy).then_inc(mix_copied, 1)
                    if s == 3 and "front" in parts:
                        act.wait_ge(u_turned, u + 3)
                        wait(act, q_proj, u + 2)
                        A.activation(u_hi[:, :, :].rearrange("p k n -> p (k n)"), misc[:, 0:C], ACT.Copy).then_inc(u_hi_done, 1)
                    if s == 5 and "front" in parts:
                        act.wait_ge(q_proj, u + 3)
                        wait(act, q_ready, u + 2)
                        A.activation(q_f[:, :], misc[0:QK, 0:P], ACT.Relu, bias=bqk[:, 0:1],
                                     scale=sc[0:QK, 10:11]).then_inc(q_relu, 1)
                    if s == 7 and "prepare" in parts:
                        act.wait_ge(l_turned, i + 2)
                        wait(act, l_proj, i + 1)
                        A.activation(l_hi[:, :, :].rearrange("p k n -> p (k n)"), misc[:, 0:C], ACT.Copy).then_inc(l_hi_done, 1)
                    if s == STEPS - 1 and "peak" in parts:
                        act.wait_ge(max_turned, u + 2)
                        A.activation(q_peak[QK:P, :], misc[QK:P, 0:P], ACT.Copy).then_inc(max_rows, 1)

                def step(s):
                    n = STEPS * i + s
                    act.wait_ge(ig_ready, n + 1)
                    A.activation(cell[:, s % 2, :, :, 2], z_ig[p][:, s * 2 * S:(s + 1) * 2 * S], ACT.Tanh,
                                 scale=1.0 / Z).then_inc(ig_act, 1)
                    act.wait_ge(o_ready, n + 1)
                    A.activation(t_o[:, s % 2, :], z_o[p][:, s * S:(s + 1) * S], ACT.Tanh, scale=1.0 / Z)
                    act.wait_ge(c_ready, n + 1)
                    A.activation(t_c[:, :], scan[:, :, 3], ACT.Tanh, scale=0.5).then_inc(c_act, 1)

                for s in range(STEPS):
                    if "steps" in parts:
                        step(s)
                    piece(s)

            schedule(act, iteration)

        @block.tensor
        def _(pe):
            E = nc.tensor
            pe.wait_ge(weights_ready, 1)
            pe.wait_ge(ident_ready, 3)
            pe.wait_ge(wo_loaded, 16)

            def products(ps, pairs, start=True, stop=True):
                for n, (w, v) in enumerate(pairs):
                    last = E.matmul(ps, w, v, start=start and n == 0, stop=stop and n == len(pairs) - 1,
                                    skip_group_check=not (start and stop))
                return last

            def turn(k, p):
                g = 2 * k + p
                pe.wait_ge(g_normed, g + 1)
                wait(pe, g_lo_done, g - 1)
                for j in range(GROUP):
                    for c in range(KC):
                        last = E.transpose((z_ig, z_o)[p][c][:, j * P:(j + 1) * P], g_n[:, p, j, c * P:(c + 1) * P], ident[:, :])
                last.then_inc(g_turned, 1)

            def project(k, p):
                g = 2 * k + p
                pe.wait_ge(g_lo_done, g + 1)
                wait(pe, g_relu, g - 1)
                pairs = []
                for c in range(KC):
                    pairs += [(Wk_hi[:, c, :], g_hi[:, p, c, :]), (Wk_hi[:, c, :], g_lo[:, p, c, :]),
                              (Wk_lo[:, c, :], g_hi[:, p, c, :])]
                products((score_ps, peak_ps)[p][0:QK, :], pairs).then_inc(g_k_proj, 1)
                wait(pe, g_vals, 2 * g - 3)
                for j in range(GROUP):
                    pairs = []
                    for c in range(KC):
                        hi, lo = (a[:, p, c, j * P:(j + 1) * P] for a in (g_hi, g_lo))
                        pairs += [(hi, Wv_hi[:, c, :]), (hi, Wv_lo[:, c, :]), (lo, Wv_hi[:, c, :])]
                    last = products((misc, mix_ps)[p][:, j * D:(j + 1) * D], pairs)
                last.then_inc(g_v_proj, 1)

            def slot(k, p, after):
                if has(k, p, 1, after):
                    turn(*later(k, p, 1))
                if has(k, p, 0, after):
                    project(k, p)

            slots(pe, slot)
            pe.wait_ge(g_keys, 2 * GROUPS)
            pe.wait_ge(g_vals, 2 * GROUPS)
            pe.wait_ge(bias_moved, 16)
            pe.wait_ge(edge_rows, 16)
            pe.wait_ge(ident_ready, 7)

            def iteration(k, p, parts):
                u = 2 * k + p
                q = 1 - p
                i = u - AHEAD

                def mix(v, r, c, tiles):
                    for j in tiles:
                        t = c * SUB + j
                        last = E.matmul(mix_ps[0:D + 1, 0:P], u_v[:, r, t, :], probs[:, c % 2, j * P:(j + 1) * P],
                                        start=t == 0, stop=t == BLOCKS - 1, skip_group_check=True)
                    if j == SUB - 1:
                        last.then_inc(mixed_chunk, 1)

                def piece(s):
                    if "tail" in parts and s == 0:
                        mix(u - 1, q, CHUNKS - 1, (2, 3))
                    if "mix" in parts and s in SCORE:
                        c = SCORE.index(s)
                        if c == 0:
                            pe.wait_ge(q_copied, u + 1)
                            pe.wait_ge(max_rows, u + 1)
                        wait(pe, exp_done, CHUNKS * u + c)
                        for j in range(SUB):
                            key = keys[:, bass.ds((u % B) * T + (c * SUB + j) * P, P)]
                            last = E.matmul(score_ps[:, j * P:(j + 1) * P], key, q_peak[:, :], start=True, stop=True)
                        last.then_inc(scored, 1)
                    if "mix" in parts and s > 0:
                        for c, tiles in MIX[s]:
                            if c == 0 and tiles[0] == 0:
                                pe.wait_ge(v_loaded[p], 16 * (k + 1))
                                wait(pe, mix_copied, u)
                            if tiles[0] == 0:
                                pe.wait_ge(exp_done, CHUNKS * u + c + 1)
                            mix(u, p, c, tiles)
                    if s == 0 and "output" in parts:
                        if "peak" in parts:
                            pe.wait_ge(max_rows, u + 1)
                        else:
                            pe.wait_ge(l_lo_done, i + 1 if "steps" in parts else LBLOCKS)
                            pe.wait_ge(max_rows, UNITS + 1)
                        pe.wait_ge(h_ready, STEPS * i)
                        for c in range(KC):
                            last = E.transpose(misc[:, c * P:(c + 1) * P],
                                               h_all[:, q, c, :, :].rearrange("p t b -> p (t b)"), ident[:, :])
                        last.then_inc(h_turned, 1)
                    if s in PEAK_PE and "peak" in parts:
                        c = PEAK_PE.index(s)
                        if c == 0:
                            pe.wait_ge(q_ready, u + 2)
                        wait(pe, peak_read, CHUNKS * (u + 1) + c)
                        E.matmul(peak_ps[:, :], q_stack[:, q, :], keys[:, bass.ds(((u + 1) % B) * T + c * CH, CH)],
                                 start=True, stop=True).then_inc(peak_scored, 1)
                    if s == 1 and "tail" in parts:
                        pe.wait_ge(mix_copied, u)
                        if "output" in parts:
                            pe.wait_ge(y_ready, i)
                        elif "peak" in parts:
                            pe.wait_ge(max_rows, u + 1)
                        E.matmul(misc[:, 0:P + 1], mix_t[:, :], Wo_x[:, 0:P + 1], start=True, stop=True)
                    if s == 2 and "tail" in parts:
                        E.matmul(misc[:, P + 1:C + 1], mix_t[:, :], Wo_x[:, P + 1:C + 1], start=True, stop=True).then_inc(projected, 1)
                    if s == 3 and "front" in parts:
                        pe.wait_ge(u_normed, u + 3)
                        if "tail" in parts:
                            pe.wait_ge(tail_chain, 2 * u)
                        elif "peak" in parts:
                            wait(pe, max_rows, u + 1)
                        for c in range(KC):
                            last = E.transpose(misc[:, c * P:(c + 1) * P], u_n[:, c * P:(c + 1) * P], ident[:, :])
                        last.then_inc(u_turned, 1)
                    if s == 5 and "front" in parts:
                        pe.wait_ge(u_lo_done, u + 3)
                        pairs = []
                        for c in range(KC):
                            pairs += [(Wq_hi[:, c, :], u_hi[:, c, :]), (Wq_hi[:, c, :], u_lo[:, c, :]),
                                      (Wq_lo[:, c, :], u_hi[:, c, :])]
                        products(misc[0:QK, 0:P], pairs).then_inc(q_proj, 1)
                    if s == 7 and "prepare" in parts:
                        pe.wait_ge(l_normed, i + 2)
                        if "front" in parts:
                            pe.wait_ge(q_relu, u + 3)
                        elif "tail" in parts:
                            pe.wait_ge(tail_chain, 2 * u)
                        if "output" in parts:
                            pe.wait_ge(y_ready, i)
                        for c in range(KC):
                            last = E.transpose(misc[:, c * P:(c + 1) * P], l_n[:, c * P:(c + 1) * P], ident[:, :])
                        last.then_inc(l_turned, 1)
                    if s in GATE_PE and "prepare" in parts:
                        first = sum(count for step_before, count in GATE_PE.items() if step_before < s)
                        if first == 0:
                            pe.wait_ge(l_lo_done, i + 2)
                        for m in range(first, first + GATE_PE[s]):
                            j, c = m // 7, (m % 7 - 1) // 3
                            zb, per, g = (z_ig[q], 2 * S, j) if j < 4 else (z_o[q], S, j - 4)
                            area = zb[:, 0:STEPS * per].rearrange("p (s c) -> p s c", c=per)[:, :, g * B:(g + 1) * B]
                            w = slice(j * P, (j + 1) * P)
                            if m % 7 == 0:
                                pair = (bias_parts[:, w], ones2[:, :])
                            else:
                                pair = ((U_hi[:, c, w], l_hi[:, c, :]), (U_hi[:, c, w], l_lo[:, c, :]),
                                        (U_lo[:, c, w], l_hi[:, c, :]))[(m % 7 - 1) % 3]
                            last = E.matmul(area, *pair, start=m in (0, 28), stop=False, skip_group_check=True)
                        if m == 41:
                            last.then_inc(l_proj, 1)
                    if s == STEPS - 1 and "peak" in parts:
                        pe.wait_ge(max_ready, u + 2)
                        if "prepare" in parts:
                            pe.wait_ge(l_lo_done, i + 2)
                        if "front" in parts:
                            pe.wait_ge(q_relu, u + 3)
                        E.transpose(misc[:, 0:P], max_cols[:, :], ident[:, :]).then_inc(max_turned, 1)

                def step(s):
                    n = STEPS * i + s

                    def part(j, c, w, h):
                        zb, col = (z_ig[p], s * 2 * S + j * B) if j < 4 else (z_o[p], s * S + (j - 4) * B)
                        return E.matmul(zb[:, col:col + B], w[:, c, j * P:(j + 1) * P], h[:, c * B:(c + 1) * B],
                                        start=False, stop=False, skip_group_check=True)

                    pe.wait_ge(h_hi_ready, n + 1)
                    for j in range(4):
                        for c in range(KC):
                            part(j, c, V_lo, h_hi)
                    for j in range(2):
                        for c in range(KC):
                            part(j, c, V_hi, h_hi)
                    pe.wait_ge(h_lo_ready, n + 1)
                    for j in range(4):
                        for c in range(KC):
                            if j >= 2:
                                part(j, c, V_hi, h_hi)
                            last = part(j, c, V_hi, h_lo)
                    last.then_inc(ig_ready, 1)
                    for j in range(4, 6):
                        for c in range(KC):
                            part(j, c, V_lo, h_hi)
                            part(j, c, V_hi, h_hi)
                            last = part(j, c, V_hi, h_lo)
                    last.then_inc(o_ready, 1)

                for s in range(STEPS):
                    if "steps" in parts:
                        step(s)
                    piece(s)

            schedule(pe, iteration)


_INS = ['x', 'L0_conv_Wq', 'L0_conv_bq', 'L0_conv_Wk', 'L0_conv_bk', 'L0_conv_Wv', 'L0_conv_bv', 'L0_conv_Wo', 'L0_conv_bo',
        'L0_ffn_U_i', 'L0_ffn_V_i', 'L0_ffn_b_i', 'L0_ffn_U_f', 'L0_ffn_V_f', 'L0_ffn_b_f', 'L0_ffn_U_c', 'L0_ffn_V_c',
        'L0_ffn_b_c', 'L0_ffn_U_o', 'L0_ffn_V_o', 'L0_ffn_b_o']


def kernel(**inputs):
    import numpy as _np
    import concourse.bacc as _bacc
    from concourse import mybir as _mybir
    from concourse.bass_utils import run_bass_kernel_spmd as _run

    nc = _bacc.Bacc("TRN2", target_bir_lowering=False, num_devices=1)
    arrays, args = {}, []
    for name in _INS:
        a = _np.ascontiguousarray(inputs[name])
        arrays[f"in_{name}_dram"] = a
        args.append(nc.dram_tensor(f"in_{name}_dram", a.shape, _mybir.dt.from_np(a.dtype), kind="ExternalInput").ap())
    shape = inputs["x"].shape
    args.append(nc.dram_tensor("out_0_dram", shape, _mybir.dt.float32, kind="ExternalOutput").ap())
    metaformer_layer(nc, *args)
    r = _run(nc, [arrays], core_ids=[0])
    return r.results[0]["out_0_dram"]
```
